# Optimizing a Trainium2 kernel written in Bass

```python
import numpy as np
import jax
import jax.numpy as jnp

def _softmax(x, axis=-1):
    return jax.nn.softmax(x, axis=axis)

def _gelu(x):
    return jax.nn.gelu(x, approximate=True)

def _silu(x):
    return jax.nn.silu(x)

def _sigmoid(x):
    return jax.nn.sigmoid(x)

def _layernorm(x, axis=-1, eps=1e-05):
    m = jnp.mean(x, axis=axis, keepdims=True)
    v = jnp.var(x, axis=axis, keepdims=True)
    return (x - m) / jnp.sqrt(v + eps)

def _scatter_add(tgt, idx, src, axis=0):
    return tgt.at[idx].add(src)

def _segment_sum(src, seg, n):
    return jax.ops.segment_sum(src, seg, n)
kernel_name = 'mk_seq_preln_d2_jaxref_r8_d79041'

def setup_inputs(seed: int=0):
    np.random.seed(seed)
    _w = jnp.asarray

    def _L0_attn_setup():
        import jax, jax.numpy as jnp
        import numpy as np
        N_HEADS = 16
        WINDOW = 128
        EPS = 1e-06
        NEG_INF = -1e+30

        def _l2norm(t):
            n = jnp.sqrt(jnp.sum(t * t, axis=-1, keepdims=True))
            return t / jnp.maximum(n, EPS)
        key = jax.random.key(seed)
        ks = jax.random.split(key, 5)
        B, T, D = (2, 256, 128)
        scale = 1.0 / np.sqrt(D)
        return {'x': jax.random.normal(ks[0], (B, T, D), dtype=jnp.float32), 'Wq': jax.random.normal(ks[1], (D, D), dtype=jnp.float32) * scale, 'Wk': jax.random.normal(ks[2], (D, D), dtype=jnp.float32) * scale, 'Wv': jax.random.normal(ks[3], (D, D), dtype=jnp.float32) * scale, 'Wo': jax.random.normal(ks[4], (D, D), dtype=jnp.float32) * scale}
    _L0_attn_in = _L0_attn_setup()

    def _L0_ffn_setup():
        import jax, jax.numpy as jnp
        import numpy as np
        S, B, H, I, E = (64, 2, 128, 352, 8)
        key = jax.random.key(seed)
        ks = jax.random.split(key, 5)
        return {'hidden_states': jax.random.normal(ks[0], (S, B, H), dtype=jnp.float32), 'router_w': jax.random.normal(ks[1], (E, H), dtype=jnp.float32) * 0.02, 'gate_w': jax.random.normal(ks[2], (E, I, H), dtype=jnp.float32) * 0.02, 'up_w': jax.random.normal(ks[3], (E, I, H), dtype=jnp.float32) * 0.02, 'down_w': jax.random.normal(ks[4], (E, H, I), dtype=jnp.float32) * 0.02}
    _L0_ffn_in = _L0_ffn_setup()

    def _L1_attn_setup():
        import jax, jax.numpy as jnp
        import numpy as np
        H = 16
        DH = 64
        M = 32
        ITERS = 6
        K = 13

        def moore_penrose_inverse(a, iters=ITERS):
            a_abs = jnp.abs(a)
            col = a_abs.sum(axis=-1)
            row = a_abs.sum(axis=-2)
            z = jnp.swapaxes(a, -1, -2) / (jnp.max(col) * jnp.max(row))
            I = jnp.eye(a.shape[-1], dtype=a.dtype)
            for _ in range(iters):
                az = a @ z
                z = 0.25 * z @ (13 * I - az @ (15 * I - az @ (7 * I - az)))
            return z
        key = jax.random.key(seed)
        k1, k2, k3, k4 = jax.random.split(key, 4)
        b, n, dim = (4, 512, 128)
        inner = H * DH
        x = jax.random.normal(k1, (b, n, dim), dtype=jnp.float32)
        w_qkv = jax.random.normal(k2, (dim, 3 * inner), dtype=jnp.float32) * 0.02
        w_conv = jax.random.normal(k3, (H, 1, K, 1), dtype=jnp.float32) * 0.1
        w_fc = jax.random.normal(k4, (inner, dim), dtype=jnp.float32) * 0.02
        b_fc = jnp.zeros((dim,), dtype=jnp.float32)
        return {'x': x, 'w_qkv': w_qkv, 'w_conv': w_conv, 'w_fc': w_fc, 'b_fc': b_fc}
    _L1_attn_in = _L1_attn_setup()

    def _L1_ffn_setup():
        import jax, jax.numpy as jnp
        import numpy as np
        DIM = 128
        INTER = 64
        E = 8
        TOP_K = 2
        ROUTE_SCALE = 1.0
        key = jax.random.key(seed)
        ks = jax.random.split(key, 8)
        s_d = 1.0 / np.sqrt(DIM)
        s_f = 1.0 / np.sqrt(INTER)
        x = jax.random.normal(ks[0], (2, 256, DIM), dtype=jnp.float32)
        gate_w = jax.random.uniform(ks[1], (E, DIM), jnp.float32, -s_d, s_d)
        wg = jax.random.uniform(ks[2], (E, INTER, DIM), jnp.float32, -s_d, s_d)
        wu = jax.random.uniform(ks[3], (E, INTER, DIM), jnp.float32, -s_d, s_d)
        wd = jax.random.uniform(ks[4], (E, DIM, INTER), jnp.float32, -s_f, s_f)
        sg = jax.random.uniform(ks[5], (INTER, DIM), jnp.float32, -s_d, s_d)
        su = jax.random.uniform(ks[6], (INTER, DIM), jnp.float32, -s_d, s_d)
        sd = jax.random.uniform(ks[7], (DIM, INTER), jnp.float32, -s_f, s_f)
        return {'x': x, 'gate_w': gate_w, 'wg': wg, 'wu': wu, 'wd': wd, 'sg': sg, 'su': su, 'sd': sd}
    _L1_ffn_in = _L1_ffn_setup()
    _d = {'L0_attn_x': _L0_attn_in['x'], 'L0_attn_Wq': _L0_attn_in['Wq'], 'L0_attn_Wk': _L0_attn_in['Wk'], 'L0_attn_Wv': _L0_attn_in['Wv'], 'L0_attn_Wo': _L0_attn_in['Wo'], 'L0_ffn_router_w': _L0_ffn_in['router_w'], 'L0_ffn_gate_w': _L0_ffn_in['gate_w'], 'L0_ffn_up_w': _L0_ffn_in['up_w'], 'L0_ffn_down_w': _L0_ffn_in['down_w'], 'L1_attn_w_qkv': _L1_attn_in['w_qkv'], 'L1_attn_w_conv': _L1_attn_in['w_conv'], 'L1_attn_w_fc': _L1_attn_in['w_fc'], 'L1_attn_b_fc': _L1_attn_in['b_fc'], 'L1_ffn_gate_w': _L1_ffn_in['gate_w'], 'L1_ffn_wg': _L1_ffn_in['wg'], 'L1_ffn_wu': _L1_ffn_in['wu'], 'L1_ffn_wd': _L1_ffn_in['wd'], 'L1_ffn_sg': _L1_ffn_in['sg'], 'L1_ffn_su': _L1_ffn_in['su'], 'L1_ffn_sd': _L1_ffn_in['sd']}
    _x0 = _d['L0_attn_x']
    _d['L0_attn_x'] = jax.random.normal(jax.random.fold_in(jax.random.key(seed), 1), (1, 2048, 128), dtype=_x0.dtype)
    del _x0
    return _d

def reference(L0_attn_x, L0_attn_Wq, L0_attn_Wk, L0_attn_Wv, L0_attn_Wo, L0_ffn_router_w, L0_ffn_gate_w, L0_ffn_up_w, L0_ffn_down_w, L1_attn_w_qkv, L1_attn_w_conv, L1_attn_w_fc, L1_attn_b_fc, L1_ffn_gate_w, L1_ffn_wg, L1_ffn_wu, L1_ffn_wd, L1_ffn_sg, L1_ffn_su, L1_ffn_sd):

    def _L0_attn_ref(x, Wq, Wk, Wv, Wo):
        import jax, jax.numpy as jnp
        import numpy as np
        N_HEADS = 16
        WINDOW = 128
        EPS = 1e-06
        NEG_INF = -1e+30

        def _l2norm(t):
            n = jnp.sqrt(jnp.sum(t * t, axis=-1, keepdims=True))
            return t / jnp.maximum(n, EPS)
        B, T, D = x.shape
        H, hd = (N_HEADS, D // N_HEADS)

        def proj(W):
            return jnp.einsum('btd,ed->bte', x, W).reshape(B, T, H, hd).transpose(0, 2, 1, 3)
        q = _l2norm(proj(Wq))
        k = _l2norm(proj(Wk))
        v = proj(Wv)
        attn = jnp.einsum('bhqd,bhkd->bhqk', q, k)
        pos = jnp.arange(T)
        rel = pos[None, :] - pos[:, None]
        mask = (rel < 0) | (rel >= WINDOW)
        base = jnp.linspace(0.0, 1.0, H, dtype=x.dtype)
        slopes = jnp.power(jnp.asarray(2.0, x.dtype), -(8.0 * base))
        alibi = -jnp.abs(rel).astype(x.dtype)[None, :, :] * slopes[:, None, None]
        bias = jnp.where(mask[None, :, :], jnp.asarray(NEG_INF, x.dtype), alibi)
        attn = jax.nn.softmax(attn + bias[None], axis=-1)
        out = jnp.einsum('bhqk,bhkd->bhqd', attn, v)
        out = out.transpose(0, 2, 1, 3).reshape(B, T, D)
        return jnp.einsum('btd,ed->bte', out, Wo)

    def _L0_ffn_ref(hidden_states, router_w, gate_w, up_w, down_w):
        import jax, jax.numpy as jnp
        import numpy as np
        S, B, H, I, E = (64, 2, 128, 352, 8)
        router_logits = jnp.einsum('sbh,eh->sbe', hidden_states, router_w)
        routing_indices = jnp.argmax(router_logits, axis=-1)
        out = jnp.zeros_like(hidden_states)
        for e in range(E):
            mask = (routing_indices == e)[..., None]
            xe = jnp.where(mask, hidden_states, 0.0)
            g = jnp.einsum('sbh,ih->sbi', xe, gate_w[e])
            u = jnp.einsum('sbh,ih->sbi', xe, up_w[e])
            ye = jnp.einsum('sbi,hi->sbh', jax.nn.silu(g) * u, down_w[e])
            out = out + jnp.where(mask, ye, 0.0)
        return out

    def _L1_attn_ref(x, w_qkv, w_conv, w_fc, b_fc):
        import jax, jax.numpy as jnp
        import numpy as np
        H = 16
        DH = 64
        M = 32
        ITERS = 6
        K = 13

        def moore_penrose_inverse(a, iters=ITERS):
            a_abs = jnp.abs(a)
            col = a_abs.sum(axis=-1)
            row = a_abs.sum(axis=-2)
            z = jnp.swapaxes(a, -1, -2) / (jnp.max(col) * jnp.max(row))
            I = jnp.eye(a.shape[-1], dtype=a.dtype)
            for _ in range(iters):
                az = a @ z
                z = 0.25 * z @ (13 * I - az @ (15 * I - az @ (7 * I - az)))
            return z
        b, n, dim = x.shape
        scale = DH ** (-0.5)
        qkv = x @ w_qkv
        q, k, v = jnp.split(qkv, 3, axis=-1)
        split_heads = lambda t: t.reshape(b, n, H, DH).transpose(0, 2, 1, 3)
        q, k, v = (split_heads(q) * scale, split_heads(k), split_heads(v))
        l = n // M
        q_l = q.reshape(b, H, M, l, DH).sum(axis=3) / l
        k_l = k.reshape(b, H, M, l, DH).sum(axis=3) / l
        sim1 = jnp.einsum('bhid,bhjd->bhij', q, k_l)
        sim2 = jnp.einsum('bhid,bhjd->bhij', q_l, k_l)
        sim3 = jnp.einsum('bhid,bhjd->bhij', q_l, k)
        attn1 = jax.nn.softmax(sim1, axis=-1)
        attn2 = jax.nn.softmax(sim2, axis=-1)
        attn3 = jax.nn.softmax(sim3, axis=-1)
        attn2_inv = moore_penrose_inverse(attn2)
        out = attn1 @ attn2_inv @ (attn3 @ v)
        res = jax.lax.conv_general_dilated(out, w_conv, window_strides=(1, 1), padding=((K // 2, K // 2), (0, 0)), feature_group_count=H, dimension_numbers=('NCHW', 'OIHW', 'NCHW'))
        out = out + res
        out = out.transpose(0, 2, 1, 3).reshape(b, n, H * DH)
        out = out @ w_fc + b_fc
        return out

    def _L1_ffn_ref(x, gate_w, wg, wu, wd, sg, su, sd):
        import jax, jax.numpy as jnp
        import numpy as np
        DIM = 128
        INTER = 64
        E = 8
        TOP_K = 2
        ROUTE_SCALE = 1.0
        B, S, D = x.shape
        xf = x.reshape(-1, D)
        N = xf.shape[0]
        scores = jax.nn.softmax(xf @ gate_w.T, axis=-1)
        _, idx = jax.lax.top_k(scores, TOP_K)
        weights = jnp.take_along_axis(scores, idx, axis=-1) * ROUTE_SCALE
        cw = jnp.zeros((N, E), dtype=xf.dtype)
        cw = cw.at[jnp.arange(N)[:, None], idx].add(weights)
        g = jnp.einsum('nd,efd->nef', xf, wg)
        u = jnp.einsum('nd,efd->nef', xf, wu)
        h = jax.nn.silu(g) * u
        y = jnp.einsum('nef,edf->ned', h, wd)
        routed = jnp.einsum('ned,ne->nd', y, cw)
        shared = jax.nn.silu(xf @ sg.T) * (xf @ su.T) @ sd.T
        return (routed + shared).reshape(B, S, D)
    x = L0_attn_x
    x = x + _L0_attn_ref(_layernorm(x, axis=-1), L0_attn_Wq, L0_attn_Wk, L0_attn_Wv, L0_attn_Wo)
    x = x + _L0_ffn_ref(_layernorm(x, axis=-1), L0_ffn_router_w, L0_ffn_gate_w, L0_ffn_up_w, L0_ffn_down_w)
    x = x + _L1_attn_ref(_layernorm(x, axis=-1), L1_attn_w_qkv, L1_attn_w_conv, L1_attn_w_fc, L1_attn_b_fc)
    x = x + _L1_ffn_ref(_layernorm(x, axis=-1), L1_ffn_gate_w, L1_ffn_wg, L1_ffn_wu, L1_ffn_wd, L1_ffn_sg, L1_ffn_su, L1_ffn_sd)
    return x

_drawn_inputs = setup_inputs


def setup_inputs(seed=0):
    import zlib

    import numpy as np

    out = dict(_drawn_inputs(seed))
    spreads = {'L1_attn_b_fc': (0.0, 0.1)}
    factors = {'L0_ffn_router_w': 6.327,
     'L0_ffn_gate_w': 6.025,
     'L0_ffn_up_w': 5.964,
     'L0_ffn_down_w': 5.977,
     'L1_attn_w_qkv': 8.0,
     'L1_attn_w_conv': 8.0,
     'L1_attn_w_fc': 8.0,
     'L1_ffn_gate_w': 6.249,
     'L1_ffn_wg': 5.493,
     'L1_ffn_wu': 5.4,
     'L1_ffn_wd': 5.325,
     'L1_ffn_sg': 8.0,
     'L1_ffn_su': 8.0,
     'L1_ffn_sd': 8.0}
    for name, (base, spread) in spreads.items():
        noise = np.random.default_rng([zlib.crc32(name.encode()), seed]).standard_normal(out[name].shape)
        drawn = base * np.exp(spread * noise) if base else spread * noise
        out[name] = jnp.asarray(drawn.astype(out[name].dtype))
    for name, factor in factors.items():
        out[name] = (out[name] * factor).astype(out[name].dtype)
    return out
```

```python
from contextlib import ExitStack

import concourse.bass as bass
from concourse import mybir

ALU = mybir.AluOpType
ACT = mybir.ActivationFunctionType
AX = mybir.AxisListType.X
F32 = mybir.dt.float32
BF16 = mybir.dt.bfloat16
I32 = mybir.dt.int32

NT = 16
NS = 32
NTS = 23


class Queues:

    def __init__(self, nc, ctx):
        self.nc, self.ctx = nc, ctx
        self.lists = {k: [] for k in ("tensor", "vector", "scalar", "gpsimd", "sync")}
        self.sems, self.count = {}, {}

    def sem(self, name):
        if name not in self.sems:
            self.sems[name] = self.ctx.enter_context(self.nc.semaphore("s_" + name))
            self.count[name] = 0
        return self.sems[name]

    def op(self, engine, fn, waits=(), s=None, by=1):
        token = None
        if s is not None:
            self.sem(s)
            self.count[s] += by
            token = (s, self.count[s])
        self.lists[engine].append((fn, [w for w in waits if w is not None], s, by))
        return token

    def pe(self, fn, w=(), s=None):
        return self.op("tensor", fn, w, s)

    def dve(self, fn, w=(), s=None):
        return self.op("vector", fn, w, s)

    def act(self, fn, w=(), s=None):
        return self.op("scalar", fn, w, s)

    def pool(self, fn, w=(), s=None):
        return self.op("gpsimd", fn, w, s)

    def dma(self, out, in_, w=(), s=None, eng="sync"):
        return self.op(eng, lambda e: e.dma_start(out, in_), w, s, 16)

    def emit(self, engine, e):
        seen = {}
        for fn, waits, s, by in self.lists[engine]:
            for name, value in waits:
                if seen.get(name, 0) < value:
                    e.wait_ge(self.sems[name], value)
                    seen[name] = value
            ins = fn(e)
            if s is not None and ins is not None:
                ins.then_inc(self.sems[s], by)


def build(nc, t, out, STOP=99):
    with ExitStack() as ctx:
        q = Queues(nc, ctx)

        def sb(name, words, parts=128, dt=F32):
            return ctx.enter_context(nc.sbuf_tensor(name, [parts, words], dt))

        t = dict(t)
        xs = nc.dram_tensor("xs", (NTS * 128, 129), F32, kind="Internal").ap()
        ys = nc.dram_tensor("ys", (2048 + NTS * 128, 128), F32, kind="Internal").ap()
        PSA = ctx.enter_context(nc.psum_tensor("ps", [128, 4096], F32))
        PS = [PSA[:, 512 * i:512 * i + 512] for i in range(8)]

        X = sb("X", 2048)
        XN = sb("XN", 2048)
        XNT = sb("XNT", 2048)
        RA = sb("RA", 16384)
        RB = sb("RB", 8192)
        RC = sb("RC", NS * 8 * 18 + 16)
        RD = sb("RD", 4096)
        RE = sb("RE", 4096)
        RP = sb("RP", 6144)
        ident = sb("ident", 128)
        identb = sb("identb", 128, dt=BF16)
        wqk = sb("wqk", 256)
        wv = sb("wv", 128)
        wo = sb("wo", 128)
        mask = sb("mask", 128)
        st = sb("st", 16 * 6)
        mv = sb("mv", 32)
        sd = sb("sd", 16)
        rs = sb("rs", 16)
        nt = sb("nt", 16)
        LGS = sb("LGS", 128)
        ss = RD[:, 2048:2560]
        rn = RD[:, 2560:3072]
        sm = sb("sm", 1320)
        zero = sb("zero", 129)
        rt = sb("rt", 8)
        cst = sb("cst", 360)
        tri = sb("tri", 256, dt=BF16)
        bfc = sb("bfc", 128)
        POS = sb("POS", 16, dt=I32)
        EID = sb("EID", NTS + 1, parts=1, dt=I32)[:, 0:NTS]

        Xv = X[:, :].rearrange("p (c d) -> p c d", d=128)
        XNv = XN[:, :].rearrange("p (c d) -> p c d", d=128)
        XNTv = XNT[:, :].rearrange("p (c d) -> p c d", d=128)

        def load_x(g):
            return q.dma(Xv[:, 4 * g:4 * g + 4, :],
                         t["x"].rearrange("(c p) d -> p c d", p=128)[:, 4 * g:4 * g + 4, :], s=f"ldx{g}")

        ld_x = [load_x(0)]
        ld_id = q.dma(ident[:, :], t["ident"], s="ldid")
        ld_w = q.dma(wqk[:, :], t["wqk"], s="ldw")
        ld_w = q.dma(wv[:, :], t["wv"], s="ldw")
        ld_x += [load_x(1), load_x(2), load_x(3)]
        ld_w = q.dma(wo[:, :], t["wo"], s="ldw")
        ld_w = q.dma(mask[:, :], t["mask"], s="ldw")
        Sb = [RP[:, 3072 + 1024 * k:3072 + 1024 * (k + 1)].bitcast(BF16).rearrange(
            "p (w h f) -> p w h f", w=2, h=16) for k in range(3)]
        Sc = RP[:, 0:1536].rearrange("p (k w h f) -> p k w h f", k=3, w=2, h=16)
        ld_s0 = q.dma(RP[:, 0:1536], t["stack"], s="lds")
        ld_t0 = q.dma(RP[:, 2560:2816], t["tri"], s="ldt0")

        ld_r = q.dma(rt[:, :], t["rt"], s="ldr")
        ld_c = q.dma(cst[:, :], t["cst"], s="ldr")

        def layernorm_stats(c, w):
            a = q.dve(lambda e: e.bn_stats(st[:, 6 * c:6 * c + 6], Xv[:, c, :]), w, s="bn")
            return q.dve(lambda e: e.bn_aggr(mv[:, 2 * c:2 * c + 2], st[:, 6 * c:6 * c + 6]), [a], s="bn")

        def layernorm_scale(a, b, w):
            v = mv[:, :].rearrange("p (c two) -> p c two", two=2)
            x1 = q.dve(lambda e: e.tensor_scalar(sd[:, a:b], v[:, a:b, 1], 1e-5, None, ALU.add), w, s="va")
            x2 = q.act(lambda e: e.activation(sd[:, a:b], sd[:, a:b], ACT.Sqrt), [x1], s="sq")
            return q.dve(lambda e: e.reciprocal(rs[:, a:b], sd[:, a:b]), [x2], s="rs")

        def newton_steps(a, b, w):
            v = mv[:, :].rearrange("p (c two) -> p c two", two=2)
            x, y, u = sd[:, a:b], rs[:, a:b], nt[:, a:b]
            k = q.dve(lambda e: e.tensor_scalar(x, v[:, a:b, 1], 1e-5, None, ALU.add), w, s="nw")
            yield k
            k = q.dve(lambda e: e.tensor_scalar(y.bitcast(I32), x.bitcast(I32), -0.5, float(0x5f3759df),
                                                ALU.mult, ALU.add), [k], s="nw")
            yield k
            for _ in range(3):
                k = q.dve(lambda e: e.scalar_tensor_tensor(u, y, -0.5, x, ALU.mult, ALU.mult), [k], s="nw")
                yield k
                k = q.dve(lambda e: e.tensor_tensor(u, u, y, ALU.mult), [k], s="nw")
                yield k
                k = q.dve(lambda e: e.scalar_tensor_tensor(y, u, 1.5, y, ALU.add, ALU.mult), [k], s="nw")
                yield k

        def layernorm_apply(c, w, out=None):
            return q.dve(lambda e: e.tensor_scalar(XNv[:, c, :] if out is None else out, Xv[:, c, :], mv[:, 2 * c:2 * c + 1],
                                                   rs[:, c:c + 1], ALU.subtract, ALU.mult), w, s="xn")

        QK = RE[:, :].rearrange("p (c f) -> p c f", c=16)
        VB = RC[:, 0:NS * 8 * 18].rearrange("p (s r f) -> p s r f", s=NS, r=8)
        KBv = RA[:, :].bitcast(BF16).rearrange("p (r s k) -> p r s k", r=8, s=NS)
        QT = RB[:, :].bitcast(BF16).rearrange("p (r n) -> p r n", r=8)
        OT = RD[:, 0:2048].rearrange("p (i n) -> p i n", i=2)

        zr = q.pool(lambda e: e.memset(zero[:, :], 0.0), s="zr")
        z_vb = q.pool(lambda e: e.memset(RC[:, :], 0.0), [zr], s="zvb")
        o0 = q.pool(lambda e: e.memset(VB[0:64, :, :, 8:9], 1.0), [z_vb], s="zvb")
        o1 = q.pool(lambda e: e.memset(VB[64:128, :, :, 17:18], 1.0), [z_vb], s="zvb")
        z_kb = []
        for half, lo in ((0, 64), (64, 0)):
            for r in range(8):
                z = KBv[half:half + 64, r, :, lo:lo + 64].bitcast(F32)
                z_kb.append(q.pool(lambda e, z=z: e.memset(z, 0.0), [o1, z_kb[-1] if r == 0 and half else None],
                                   s="zkb"))
        xs_v = xs.rearrange("(t p) d -> p t d", p=128)
        xs_zero = q.dma(xs_v, zero[:, :].unsqueeze(1).to_broadcast([128, NTS, 129]), [zr], s="xsz")

        xn = [None] * 16
        ev = [None] * 16
        tpa = [None] * 16
        qkc = [None] * 16
        vev = [None] * 4
        ssq = [None] * 16
        sqs = [None] * 16
        nq3 = [None] * 4
        SQ = [RD[:, 0:256], RD[:, 256:512]]

        def norm0(g):
            c4 = range(4 * g, 4 * g + 4)
            stats = [layernorm_stats(c, [ld_x[g]]) for c in c4]
            sc = layernorm_scale(4 * g, 4 * g + 4, [stats[-1]])
            for c in c4:
                xn[c] = layernorm_apply(c, [sc])

        def turn0(c):
            b = PS[c % 2]
            tpa[c] = q.pe(lambda e: e.transpose(b[:, 0:128], XNv[:, c, :], ident[:, :]),
                          [xn[c], ld_id, ev[c - 2] if c >= 2 else None], s="tp")
            ev[c] = q.act(lambda e: e.activation(XNTv[:, c, :], b[:, 0:128], ACT.Copy), [tpa[c]], s="ev")

        def project0(c):
            b2 = PS[2 + c % 2]
            mm = q.pe(lambda e: e.matmul(b2[:, 0:256], XNTv[:, c, :], wqk[:, :], start=True, stop=True),
                      [ev[c], ld_w] + ([qkc[c - 2], sqs[c - 2]] if c >= 2 else []), s="mqk")
            qkc[c] = q.act(lambda e: e.activation(QK[:, c, :], b2[:, 0:256], ACT.Copy), [mm], s="qkc")
            sqs[c] = q.act(lambda e: e.activation(SQ[c % 2], b2[:, 0:256], ACT.Square),
                           [mm, ssq[c - 2] if c >= 2 else None], s="sqs")
            ssq[c] = q.dve(lambda e: e.tensor_reduce(ss[:, 32 * c:32 * c + 32],
                                                     SQ[c % 2].rearrange("p (h d) -> p h d", d=8), AX, ALU.add),
                           [sqs[c]], s="ssq")
            g = c // 4
            bv = PS[4 + g % 2]
            for sl in range(2):
                for half in range(2):
                    col = 64 * (2 * (c % 4) + sl)
                    vm = q.pe(lambda e, sl=sl, half=half, col=col: e.matmul(
                        bv[64 * half:64 * half + 64, col:col + 64], XNTv[:, c, 64 * sl:64 * sl + 64],
                        wv[:, 64 * half:64 * half + 64], start=True, stop=True),
                        [vev[g - 2] if g >= 2 else None], s="mv")
            if c % 4 == 3:
                for half in range(2):
                    vev[g] = q.act(lambda e, half=half: e.activation(
                        VB[64 * half:64 * half + 64, 8 * g:8 * g + 8, :, 9 * half:9 * half + 8],
                        bv[64 * half:64 * half + 64, :].rearrange("p (s r d) -> p s r d", s=8, r=8), ACT.Copy),
                        [vm, o1], s="vev")
                r = slice(128 * g, 128 * g + 128)
                nq = q.act(lambda e: e.activation(rn[:, r], ss[:, r], ACT.Sqrt), [ssq[c]], s="nq")
                nq2 = q.dve(lambda e: e.tensor_scalar(rn[:, r], rn[:, r], 1e-6, None, ALU.max), [nq], s="nq2")
                nq3[g] = q.dve(lambda e: e.reciprocal(rn[:, r], rn[:, r]), [nq2], s="nq2")

        QN = [sm[:, 256 * k:256 * k + 256] for k in range(2)]
        R1 = [sm[:, 512 + 256 * k:768 + 256 * k] for k in range(2)]
        qt_done, kb_done = [None] * 16, [None] * 16
        tq_done = [None] * 16
        tk_done = [None] * 16

        sd_done, qn_done = [None] * 16, [None] * 16

        def stack_parts(c):
            S = Sb[c % 3]
            n, r1 = QN[c % 2], R1[c % 2]
            nv = n.rearrange("p (w h d) -> p w h d", w=2, d=8)
            nf = n.rearrange("p (h d) -> p h d", d=8)
            rv = r1.rearrange("p (w h d) -> p w h d", w=2, d=8)
            rf = r1.rearrange("p (h d) -> p h d", d=8)
            Sf = S.rearrange("p w h f -> p (w h) f")
            free = [tq_done[c - 3], tk_done[c - 3]] if c >= 3 else []

            def slots(w, a, k, step):
                v = S[:, w, :, :].rearrange("p h (z d) -> p h z d", d=8)
                return v[:, :, a:a + step * (k - 1) + 1:step, :]

            def rep(v, k):
                return v.unsqueeze(2).to_broadcast([128, 16, k, 8])

            a = q.pool(lambda e: e.tensor_tensor(nf, QK[:, c, :].rearrange("p (h d) -> p h d", d=8),
                                                 rn[:, 32 * c:32 * c + 32].unsqueeze(2).to_broadcast([128, 32, 8]),
                                                 ALU.mult),
                       [z_kb[-1], nq3[c // 4], qkc[c], act_h[c - 2] if c >= 2 else None, sd_done[c - 2] if c >= 2 else None],
                       s="qn")
            yield
            act_h[c] = q.act(lambda e: e.activation(slots(0, 0, 3, 1), rep(nv[:, 0], 3), ACT.Copy),
                             [a, ld_s] + free, s="st2")
            h1 = q.dve(lambda e: e.tensor_copy(slots(1, 2, 3, 1), rep(nv[:, 1], 3)), [a, ld_s] + free, s="st1")
            yield
            b = q.dve(lambda e: e.tensor_tensor(rf, nf, Sf[:, :, 16:24], ALU.subtract), [h1, act_h[c]], s="st1")
            m1 = q.dve(lambda e: e.tensor_copy(slots(0, 3, 2, 2), rep(rv[:, 0], 2)), [b], s="st1")
            m2 = q.dve(lambda e: e.tensor_copy(slots(1, 0, 2, 5), rep(rv[:, 1], 2)), [b], s="st1")
            q.pool(lambda e: e.tensor_tensor(S[:, 0, :, 32:40], rv[:, 0], S[:, 0, :, 24:32], ALU.subtract), [m2], s="st3")
            sd_done[c] = q.pool(lambda e: e.tensor_tensor(S[:, 1, :, 8:16], rv[:, 1], S[:, 1, :, 0:8], ALU.subtract),
                                [m2], s="st3")

        def turn_queries(c):
            S = Sb[c % 3]
            bq = PS[6][:, :].bitcast(BF16)
            for r in range(8):
                tq_done[c] = q.pe(lambda e, r=r: e.transpose(
                    bq[:, 128 * r:128 * r + 128], S[:, 0, 2 * r:2 * r + 2, :].rearrange("p h f -> p (h f)"),
                    identb[:, :]), [sd_done[c], act_h[c], cp_idb, qt_done[c - 1] if c else None, *use6],
                    s="tq" if r == 7 else None)
            qt_done[c] = q.dve(lambda e: e.tensor_copy(QT[:, :, 128 * c:128 * c + 128],
                                                       bq.rearrange("p (r n) -> p r n", r=8)), [tq_done[c]], s="qt")

        def turn_keys(c):
            S = Sb[c % 3]
            bk = PS[7][:, :].bitcast(BF16)
            for r in range(8):
                tk_done[c] = q.pe(lambda e, r=r: e.transpose(
                    bk[:, 128 * r:128 * r + 128], S[:, 1, 2 * r:2 * r + 2, :].rearrange("p h f -> p (h f)"),
                    identb[:, :]), [*(kb_done[c - 1] or ()), *use7], s="tk" if r == 7 else None)
            kv = bk.rearrange("p (r s k) -> p r s k", r=8, s=2)
            k0 = q.dve(lambda e: e.tensor_copy(KBv[0:64, :, 2 * c:2 * c + 2, 0:64], kv[0:64]),
                       [tk_done[c], z_kb[-1]], s="kb0")
            k1 = q.act(lambda e: e.activation(KBv[64:128, :, 2 * c:2 * c + 2, 64:128], kv[64:128], ACT.Copy),
                       [tk_done[c], z_kb[-1]], s="kb1")
            kb_done[c] = (k0, k1)

        act_h = [None] * 16
        use6, use7 = [], []

        Pb = [RP[:, 768 * k:768 * (k + 1)].rearrange("p (j n) -> p j n", j=4) for k in range(4)]
        units = [(i, s) for s in range(NS) for i in range(2)]
        exp_done, m_dve, m_pool, pv_done = {}, {}, {}, {}
        ot_done = {}

        def lo_col(s):
            return 128 if s == 0 else 64 if s == 1 else 0

        def scores(n):
            i, s = units[n]
            bb = [PS[2 * (n % 2)], PS[2 * (n % 2) + 1]]
            lo = lo_col(s)
            w = [qt_done[s // 2], *kb_done[s // 2]]
            if n >= 2:
                w.append(exp_done[n - 2])
            elif n == 0:
                w += [qkc[15], sqs[15], ev[15], ev[14]]
            elif n == 1:
                w += [qkc[14], sqs[14]]
            for j in range(4):
                sc_ = q.pe(lambda e, j=j: e.matmul(
                    bb[j // 2][:, 192 * (j % 2) + lo:192 * (j % 2) + 192], KBv[:, 4 * i + j, s, :],
                    QT[:, 4 * i + j, 64 * (s - 2) + lo:64 * (s - 2) + 192], start=True, stop=True),
                    w, s="sc" if j == 3 else None)
            P = Pb[n % 4]
            v = PSA[:, 1024 * (n % 2):1024 * (n % 2) + 1024].rearrange("p (k z) -> p k z", k=2)[:, :, 0:384].rearrange(
                "p k (j n) -> p k j n", j=2)
            exp_done[n] = q.act(lambda e: e.activation(
                P.rearrange("p (k j) n -> p k j n", k=2)[:, :, :, lo:192], v[:, :, :, lo:192], ACT.Exp),
                [sc_, pv_done.get(n - 4)], s="exp")

        MS = (2, 1, 2, 1)

        def masks(n):
            i, s = units[n]
            P = Pb[n % 4]
            mk = mask[:, :].rearrange("p (z m) -> p z m", z=2)
            z0, z1 = (1, 2) if s < 2 else (0, 2)

            def view(a, b):
                if s < 2:
                    return P[:, a:b, 128:192].rearrange("p j m -> p j m").unsqueeze(2)
                return P[:, a:b, :].rearrange("p j (z m) -> p j z m", m=64)[:, :, 0:3:2, :]

            def mview(a, b):
                return mk[:, z0:z1, :].unsqueeze(1).to_broadcast([128, b - a, z1 - z0, 64])

            m_dve[n] = q.dve(lambda e: e.tensor_tensor(view(0, MS[n % 4]), view(0, MS[n % 4]), mview(0, MS[n % 4]), ALU.mult),
                             [exp_done[n], ld_w], s="md")
            m_pool[n] = q.pool(lambda e: e.tensor_tensor(view(MS[n % 4], 4), view(MS[n % 4], 4), mview(MS[n % 4], 4), ALU.mult),
                               [exp_done[n], ld_w], s="mp")

        z_ot = [None, None]

        def pv(n):
            i, s = units[n]
            P = Pb[n % 4]
            first_q = 64 * (s - 2)
            a = first_q + lo_col(s)
            parts = []
            while a < first_q + 192:
                b = min(first_q + 192, (a // 512 + 1) * 512)
                parts.append((a, b))
                a = b
            for a, b in parts:
                for j in range(4):
                    pv_done[n] = q.pe(lambda e, j=j, a=a, b=b: e.matmul(
                        PS[4 + i][32 * j:32 * j + 32, a % 512:a % 512 + b - a],
                        VBflat[:, 144 * s + 18 * (4 * i + j):144 * s + 18 * (4 * i + j) + 32],
                        P[:, j, a - first_q:b - first_q], start=False, stop=True, skip_group_check=True),
                        [m_dve[n], m_pool[n], z_ot[i]], s="pv" if j == 3 and b == first_q + 192 else None)
            m = (s - 5) // 4 if s >= 5 and (s - 5) % 4 == 0 else 7 if s == NS - 1 else None
            if m is not None:
                col = 256 * (m % 2)
                ot_done[m, i] = q.act(lambda e: e.activation(
                    OT[:, i, 256 * (m % 4):256 * (m % 4) + 256], PS[4 + i][:, col:col + 256], ACT.Copy),
                    [pv_done[n], tpo.get(2 * m - 7)], s="ot")
                z_ot[i] = q.dve(lambda e: e.memset(PS[4 + i][:, col:col + 256], 0.0), [ot_done[m, i]], s="zot")

        VBflat = RC[:, :]
        norm0(0)
        early = [stack_parts(c) for c in range(3)]
        for c in range(16):
            if c % 4 == 2 and c < 12:
                norm0(c // 4 + 1)
            if c == 3:
                for k in range(3):
                    for w in range(2):
                        ld_s = q.dve(lambda e, k=k, w=w: e.tensor_copy(Sb[k][:, w, :, 48:64], Sc[:, k, w]), [ld_s0], s="cps")
                ld_s = q.dve(lambda e: e.tensor_copy(tri[:, :], RP[:, 2560:2816]), [ld_t0], s="cps")
                cp_idb = q.dve(lambda e: e.tensor_copy(identb[:, :], ident[:, :]), [ld_id], s="idb")
            turn0(c)
            if c:
                project0(c - 1)
            if 7 <= c:
                next(early[(c - 7) // 3], None)
            if c == 11:
                turn_queries(0)
            if c == 12:
                turn_keys(0)
        z_ot[0] = q.dve(lambda e: e.memset(PS[4][:, :], 0.0), [vev[2]], s="zot")
        project0(15)
        z_ot[1] = q.dve(lambda e: e.memset(PS[5][:, :], 0.0), [vev[3]], s="zot")
        for _ in early[2]:
            pass
        turn_queries(1)
        turn_keys(1)
        x1 = [None] * 16
        tpo = {}
        OTN = [sm[:, 1024:1152], sm[:, 1152:1280], sm[:, 0:128], sm[:, 128:256]]
        RDN = [sm[:, 1280:1296], sm[:, 1296:1312], sm[:, 256:272], sm[:, 272:288]]

        def out_banks(c):
            return (PS[6], PS[7], 0) if c < 12 else (PS[c - 12], PS[c - 12], 256)

        def out_buf(c):
            return c % 2 if c < 12 else c % 4

        def turn_out(c):
            b, k = out_banks(c)[0], out_buf(c)
            w = [ot_done[c // 2, 0], ot_done[c // 2, 1], z_ot[0], z_ot[1]] if c >= 12 else [
                ot_done[c // 2, 0], ot_done[c // 2, 1]]
            w += [qt_done[min(15, c + 5)], *use6] if c < 12 else [exp_done[len(units) - 1]]
            for i in range(2):
                tpo[c] = q.pe(lambda e, i=i: e.transpose(b[:, 128 * i:128 * i + 128],
                                                         OT[:, i, 128 * (c % 8):128 * (c % 8) + 128], ident[:, :]),
                              w, s="tpo")
            v = b[:, 0:256].rearrange("p (r f) -> p r f", f=32)
            rd = q.dve(lambda e: e.reciprocal(RDN[k].rearrange("p (r z) -> p r z", z=2), v[:, :, 8:18:9]),
                       [tpo[c]], s="rdn")
            on_done[c] = q.dve(lambda e: e.tensor_tensor(
                XNv[:, c, :].rearrange("p (r z d) -> p r z d", r=8, z=2),
                v[:, :, 0:18].rearrange("p r (z k) -> p r z k", z=2)[:, :, :, 0:8],
                RDN[k].rearrange("p (r z) -> p r z", z=2).unsqueeze(3).to_broadcast([128, 8, 2, 8]), ALU.mult),
                [rd], s="onn")
            if c < 12:
                use6[:] = [on_done[c]]

        def turn_heads(c):
            _, b, col = out_banks(c)
            tpn_done[c] = q.pe(lambda e: e.transpose(b[:, col:col + 128], XNv[:, c, :], ident[:, :]),
                               [on_done[c], *use7, *kb_done[min(15, c + 5)]], s="tpn")
            otn[c] = q.act(lambda e: e.activation(OTN[out_buf(c)], b[:, col:col + 128], ACT.Copy), [tpn_done[c]], s="otn")
            if c < 12:
                use7[:] = [otn[c]]

        def output(c):
            _, b, col = out_banks(c)
            o = b[:, col + 128:col + 256]
            mm = q.pe(lambda e: e.matmul(o, OTN[out_buf(c)], wo[:, :], start=True, stop=True),
                      [otn[c]], s="mwo")
            x1[c] = q.dve(lambda e: e.tensor_tensor(Xv[:, c, :], o, Xv[:, c, :], ALU.add), [mm], s="x1")
            if c < 12:
                use7[:] = [x1[c]]
            st1[c] = layernorm_stats(c, [x1[c]])
            if c % 4 == 3:
                later.append(norms(c // 4))

        def norms(g):
            for k in newton_steps(4 * g, 4 * g + 4, [st1[4 * g + 3]]):
                yield
            for d in range(4 * g, 4 * g + 4):
                xn1[d] = layernorm_apply(d, [k, sd_done[min(15, d + 2)]], XE[:, d, 0:128])
                normed.append(d)
                yield

        def step_norms(steps):
            while steps and later:
                if next(later[0], "end") == "end":
                    later.pop(0)
                steps -= 1

        def turn_norm(c, bank=6, col=256, w=()):
            b = PS[bank]
            tp = q.pe(lambda e: e.transpose(b[:, col:col + 128], XE[:, c, 0:128], ident[:, :]),
                      [xn1[c], *(use6 if bank == 6 else ()), *w], s="tp")
            tv1[c] = q.act(lambda e: e.activation(XNTv[:, c, :], b[:, col:col + 128], ACT.Copy), [tp], s="ev")
            if bank == 6:
                use6.append(tv1[c])

        def route(c):
            rmm[c] = q.pe(lambda e: e.matmul(PS[6][:, 384:392], XNTv[:, c, :], rt[:, :],
                                             start=True, stop=True), [tv1[c], ld_c, *use6], s="rmm")
            lgc[c] = q.dve(lambda e: e.tensor_copy(LGS[:, 8 * c:8 * c + 8], PS[6][:, 384:392]), [rmm[c]], s="lgc")
            use6.append(lgc[c])

        XE = RE[:, 0:16 * 129].rearrange("p (c d) -> p c d", d=129)
        on_done, tpn_done, otn, st1, xn1, tv1, rmm, lgc = ({} for _ in range(8))
        later, normed, routed = [], [], []
        LAG = 3
        parts = None
        for n in range(len(units) + LAG):
            if n < len(units):
                scores(n)
            if 1 <= n <= len(units):
                masks(n - 1)
            c, k = n // 4, n % 4
            if n < len(units) and c + 3 < 16:
                if k == 0:
                    parts = stack_parts(c + 3)
                if k < 3:
                    next(parts, None)
            if n < len(units) and c + 2 < 16:
                if k == 1:
                    turn_queries(c + 2)
                if k == 3:
                    turn_keys(c + 2)
            t_ = c - 4
            if 0 <= t_ < 12:
                if k == 0:
                    turn_out(t_)
                    if routed:
                        route(routed.pop(0))
                    if normed:
                        routed.append(normed.pop(0))
                        turn_norm(routed[-1])
                if k == 1:
                    turn_heads(t_)
                if k == 2:
                    output(t_)
            if n >= LAG:
                pv(n - LAG)
            if n == 54:
                xe_id = q.dve(lambda e: e.tensor_copy(XE[:, :, 128], cst[:, 320:336]), [sd_done[15], ld_c], s="zc")
            step_norms(1)
        def turn_norms(four, bank, w):
            f = four[0]
            for c in four:
                tp = q.pe(lambda e, c=c: e.transpose(PS[bank][:, 128 * (c - f):128 * (c - f) + 128],
                                                     XE[:, c, 0:128], ident[:, :]), [xn1[c], *w], s="tp")
            tve = q.act(lambda e: e.activation(XNT[:, 128 * f:128 * f + 128 * len(four)],
                                               PS[bank][:, 0:128 * len(four)], ACT.Copy), [tp], s="ev")
            for c in four:
                tv1[c] = tve

        def logits(four):
            for c in four:
                rmm[c] = q.pe(lambda e, c=c: e.matmul(PS[7][:, 8 * c:8 * c + 8], XNTv[:, c, :], rt[:, :],
                                                      start=True, stop=True), [tv1[c], ld_c, *use7], s="rmm")

        for c in range(12, 16):
            turn_out(c)
            step_norms(3)
        step_norms(99)
        rest = normed[:]
        for c in range(12, 16):
            turn_heads(c)
        for c in routed:
            route(c)
        turn_norms(rest[:4], 4, z_ot)
        for c in range(12, 16):
            output(c)
        if len(rest) > 4:
            turn_norms(rest[4:], 5, z_ot)
        logits(rest)
        step_norms(99)
        last4 = list(range(12, 16))
        turn_norms(last4, 6, [*use6])
        logits(last4)
        lgc[15] = q.dve(lambda e: e.tensor_copy(LGS[:, 8 * rest[0]:128], PS[7][:, 8 * rest[0]:128]), [rmm[15]], s="lgc")
        last = x1[15]

        ys_v = ys[0:2048, :].rearrange("(c p) d -> p c d", p=128)
        GU = RA[:, 0:5632].rearrange("p (e n) -> p e n", e=8)
        DW = RB[:, 0:3072].rearrange("p (e k n) -> p e k n", e=8, k=3)
        ld_dw = q.dma(RB[:, 0:3072], t["dw"], [exp_done[len(units) - 1]], s="lddw")
        ld_gu = q.dma(RA[:, 0:5632], t["gu"], [exp_done[len(units) - 1]], s="ldgu")
        WV = RB[:, 7168:8192]
        MM = [RA[:, 11264 + 2048 * k:13312 + 2048 * k].rearrange("p (j c d) -> p j c d", j=4, c=4) for k in range(2)]
        WqT = RB[0:64, 3072:5120].rearrange("p (h d) -> p h d", h=16)
        WkT = RB[0:64, 5120:7168].rearrange("p (h d) -> p h d", h=16)
        TZ = RC[:, 0:2240].rearrange("p (h n) -> p h n", h=16)
        WF = RC[0:64, 2240:4288].rearrange("p (h d) -> p h d", h=16)
        lw = q.dma(WV, t["w1"], [pv_done[len(units) - 1]], s="ldw1")
        lw = q.dma(WqT, t["wqT"], [pv_done[len(units) - 1]], s="ldw1")
        lw = q.dma(WkT, t["wkT"], [pv_done[len(units) - 1]], s="ldw1")
        lt = q.dma(TZ, t["tz"], [pv_done[len(units) - 1]], s="ldt")
        lt = q.dma(WF, t["wf"], [pv_done[len(units) - 1]], s="ldt")
        lt = q.dma(bfc[:, :], t["bfc"], s="ldt")
        W3 = RD[:, 0:1160]
        D3 = RD[:, 1160:1800].rearrange("p (k n) -> p k n", k=5)
        lw3 = q.dma(W3, t["w3"], [tpn_done[15]], s="ldw3")
        lw3 = q.dma(RD[:, 1160:1800], t["d3"], [tpn_done[15]], s="ldw3")

        tz_, me = [None], [None] * 4

        def ffn0(last):
            F = RP
            OH = F[:, 0:64].bitcast(BF16)
            val, mx, m2 = F[:, 64:192], F[:, 192:208], F[:, 208:224]
            TT, PD, EB = F[:, 224:352], F[:, 352:360], F[:, 360:376]
            EN, BA = EB[:, 0:8], EB[:, 8:16]
            pi, ei = POS[:, :], EID[:, :]
            ev8 = F[0:1, 376:376 + 8 * NTS]
            onesb = tri[:, 128:256]
            lg = LGS[:, :].rearrange("p (c e) -> p c e", e=8)
            w8 = cst[:, 0:8].unsqueeze(1).to_broadcast([128, 16, 8])

            def b16(v):
                return v.unsqueeze(2).to_broadcast([128, 16, 8])

            def e3(v):
                return v.rearrange("p (c e) -> p c e", e=8)

            def ch(fn, w=()):
                chain[0] = q.dve(fn, [chain[0], *w], s="rt")
                return chain[0]

            chain = [lgc[15]]
            ch(lambda e: e.tensor_reduce(mx, lg, AX, ALU.max), [pv_done[len(units) - 1]])
            ch(lambda e: e.tensor_tensor(e3(val), lg, b16(mx), ALU.is_equal))
            ch(lambda e: e.tensor_tensor(e3(val), e3(val), w8, ALU.mult))
            ch(lambda e: e.tensor_reduce(m2, e3(val), AX, ALU.max))
            oh = ch(lambda e: e.tensor_tensor(e3(OH), w8, b16(m2), ALU.is_equal))
            for c in range(16):
                cm = q.pe(lambda e, c=c: e.matmul(PS[4][:, 0:8], onesb, OH[:, 8 * c:8 * c + 8],
                                                  start=c == 0, stop=c == 15), [oh, *z_ot], s="pm")
            q.pe(lambda e: e.matmul(PS[3][:, 0:128], tri[:, 0:128], OH, start=True, stop=True), [exp_done[len(units) - 1]])
            for c in range(15):
                pm = q.pe(lambda e, c=c: e.matmul(
                    PS[3][:, 8 * c + 8:128].rearrange("p (c e) -> p c e", e=8), onesb,
                    OH[:, 8 * c:8 * c + 8].unsqueeze(1).to_broadcast([128, 15 - c, 8]),
                    start=False, stop=True, skip_group_check=True), [], s="pm")
            big = val.rearrange("p (e k) -> p e k", e=8)
            ch(lambda e: e.tensor_tensor(big, PS[4][:, 0:8].unsqueeze(2).to_broadcast([128, 8, 16]),
                                         cst[:, 8:24].unsqueeze(1).to_broadcast([128, 8, 16]), ALU.is_gt), [cm])
            ch(lambda e: e.tensor_reduce(PD, big, AX, ALU.add))
            ch(lambda e: e.tensor_tensor(val.rearrange("p (k e) -> p k e", e=8),
                                         PD.unsqueeze(1).to_broadcast([128, 16, 8]),
                                         cst[:, 192:320].rearrange("p (k e) -> p k e", e=8), ALU.mult))
            ch(lambda e: e.tensor_reduce(EB, val.rearrange("p (k e) -> p k e", e=8), AX, ALU.add))
            ch(lambda e: e.tensor_tensor(e3(TT), e3(PS[3][:, 0:128]), BA.unsqueeze(1).to_broadcast([128, 16, 8]),
                                         ALU.add), [pm])
            ch(lambda e: e.tensor_tensor(TT, TT, OH, ALU.mult))
            ch(lambda e: e.tensor_reduce(mx, e3(TT), AX, ALU.add))
            pos = ch(lambda e: e.tensor_copy(pi, mx))
            ev3 = ev8.rearrange("p (t e) -> p t e", e=8)
            ch(lambda e: e.tensor_tensor(ev3, EN[0:1, :].unsqueeze(1).to_broadcast([1, NTS, 8]),
                                         cst[0:1, 8:8 + NTS].unsqueeze(2).to_broadcast([1, NTS, 8]), ALU.is_le))
            ch(lambda e: e.tensor_reduce(F[0:1, 880:880 + NTS], ev3, AX, ALU.add))
            eid = ch(lambda e: e.tensor_scalar(ei, F[0:1, 880:880 + NTS], 7.0, None, ALU.min))
            for c in range(16):
                scat = q.op("gpsimd", lambda e, c=c: e.indirect_dma_start(
                    out=xs, out_offset=bass.IndirectOffsetOnAxis(ap=pi[:, c:c + 1], axis=0),
                    in_=XE[:, c, :], in_offset=None), [pos, xs_zero, xe_id], "scat", 16)
            tz_[0] = q.pool(lambda e: e.tensor_tensor(TZ[:, :, 6:134], TZ[:, :, 6:134],
                                                  ident[:, :].unsqueeze(1).to_broadcast([128, 16, 128]), ALU.add),
                        [lt], s="tz")
            for k in range(2):
                for j in range(4):
                    b = PS[(0, 1, 2, 5)[j]]
                    for c in range(4):
                        h = 4 * c + j
                        lhs, rhs = (WqT, WkT) if k == 0 else (WkT, WqT)
                        mp_ = q.pe(lambda e, b=b, c=c, h=h, lhs=lhs, rhs=rhs: e.matmul(
                            b[:, 128 * c:128 * c + 128], lhs[:, h, :], rhs[:, h, :], start=True, stop=True),
                            [lw, me[j], tv1[15]], s="mp2")
                    me[j] = q.act(lambda e, b=b, j=j, k=k: e.activation(
                        MM[k][:, j, :, :], b.rearrange("p (c d) -> p c d", c=4), ACT.Copy), [mp_], s="me")
            XS = [F[:, 1024 + 516 * k:1540 + 516 * k].rearrange("p (t d) -> p t d", d=129) for k in range(2)]
            XT = [F[:, 2056 + 128 * k:2184 + 128 * k] for k in range(2)]
            SG = [F[:, 2312 + 384 * k:2312 + 384 * k + 352] for k in range(2)]
            H = [F[:, 3080 + 384 * k:3464 + 384 * k] for k in range(2)]
            HT = [F[:, 3848 + 384 * k:4232 + 384 * k] for k in range(2)]
            Y = [F[:, 4616 + 128 * k:4744 + 128 * k] for k in range(4)]
            ID = F[:, 5128:5128 + NTS].bitcast(I32)
            IDF = F[:, 5152:5156]
            hz = [q.dve(lambda e, k=k: e.memset(H[k][:, 352:384], 0.0), [tk_done[15]], s="hz") for k in range(2)]
            ld, tr, xe, gu, sg, hh, ht, he, dd, ye, yst, idc = ({} for _ in range(12))
            regs = {}

            def loads(g):
                n = min(4, NTS - 4 * g)
                k = g % 2
                ld[g] = q.dma(XS[k][:, 0:n, :], xs_v[:, 4 * g:4 * g + n, :], [scat, tr.get(4 * g - 5), idc.get(g - 2)],
                              s=f"ldxs{k}")

            def turn(n):
                g = n // 4
                if n == 0:
                    loads(0)
                if n % 4 == 0 and g + 1 < (NTS + 3) // 4:
                    loads(g + 1)
                b = PS[0]

                def expert(e):
                    regs[n] = e.value_load(ei[0:1, n:n + 1], min_val=0, max_val=7)
                q.pe(expert, [eid])
                if n % 4 == 0:
                    m = min(4, NTS - n)
                    v, u = XS[g % 2][:, 0:m, 128], IDF[:, 0:m]
                    k = q.dve(lambda e: e.scalar_tensor_tensor(u, v, 0.0, cst[:, 336 + n:336 + n + m],
                                                               ALU.is_equal, ALU.mult), [ld[g], idc.get(g - 1)], s="idc")
                    idc[g] = q.dve(lambda e: e.scalar_tensor_tensor(ID[:, n:n + m], v, -1.0, u, ALU.add, ALU.add),
                                   [k], s="idc")
                tr[n] = q.pe(lambda e: e.transpose(b[:, 0:128], XS[g % 2][:, n % 4, 0:128],
                                                   ident[:, :]), [ld[g], xe.get(n - 1), me[3]], s="trx")
                xe[n] = q.act(lambda e: e.activation(XT[n % 2], b[:, 0:128], ACT.Copy), [tr[n], gu.get(n - 2)], s="xe")

            def up(n):
                bg, bu = PS[2 + n % 2], PS[4 + n % 2]

                q.pe(lambda e: e.matmul(bg[:, 0:352], XT[n % 2], GU[:, bass.ds(regs[n], 1), 0:352], start=True, stop=True),
                     [xe[n], ld_gu, hh.get(n - 2), chain[0]])
                gu[n] = q.pe(lambda e: e.matmul(bu[:, 0:352], XT[n % 2], GU[:, bass.ds(regs[n], 1), 352:704],
                                                start=True, stop=True), s="gu")
                sg[n] = q.act(lambda e: e.activation(SG[n % 2], bg[:, 0:352], ACT.Silu), [gu[n], hh.get(n - 2)], s="sg")
                hh[n] = q.dve(lambda e: e.tensor_tensor(H[n % 2][:, 0:352], SG[n % 2], bu[:, 0:352], ALU.mult),
                              [sg[n], hz[1], ht.get(n - 2)], s="hh")

            def down(n):
                b, b2 = PS[6], PS[7]
                for k in range(3):
                    ht[n] = q.pe(lambda e, k=k: e.transpose(b[:, 128 * k:128 * k + 128],
                                                            H[n % 2][:, 128 * k:128 * k + 128], ident[:, :]),
                                 [hh[n], he.get(n - 1), x1[15]], s="ht")
                he[n] = q.dve(lambda e: e.tensor_copy(HT[n % 2], b[:, 0:384]), [ht[n], dd.get(n - 2)], s="he")

            def down2(n):
                b2 = PS[7]
                for k in range(3):
                    dd[n] = q.pe(lambda e, k=k: e.matmul(b2[:, 0:128], HT[n % 2][:, 128 * k:128 * k + 128],
                                                         DW[:, bass.ds(regs[n], 1), k, :], start=k == 0, stop=k == 2),
                                 [he[n], ye.get(n - 1), ld_dw], s="dd")
                g = n // 4
                ye[n] = q.act(lambda e: e.activation(Y[n % 4], b2[:, 0:128], ACT.Copy), [dd[n], yst.get(n - 4)], s="ye")
                yst[n] = q.op("gpsimd", lambda e: e.indirect_dma_start(
                    out=ys, out_offset=bass.IndirectOffsetOnAxis(ap=ID[:, n:n + 1], axis=0),
                    in_=Y[n % 4], in_offset=None), [ye[n], idc[g]], f"yst{n % 4}", 16)

            for n in range(NTS + 3):
                if n < NTS:
                    turn(n)
                if 1 <= n <= NTS:
                    up(n - 1)
                if 2 <= n <= NTS + 1:
                    down(n - 2)
                if n >= 3:
                    down2(n - 3)
            warm = q.act(lambda e: e.activation(nt[:, 0:1], zero[:, 0:1], ACT.Exp), [ye[NTS - 1]], s="warm")
            for g in range(4):
                gat[g] = q.dma(XNv[:, 4 * g:4 * g + 4, :], ys_v[:, 4 * g:4 * g + 4, :],
                               [*(yst[n] for n in range(NTS - 4, NTS)), *(tpn_done[c] for c in range(16)) ], s=f"gat{g}")
            stt, agg = {}, {}

            def add(g, put=q.dve, name="x2"):
                f = slice(512 * g, 512 * g + 512)
                x2[g] = put(lambda e: e.tensor_tensor(X[:, f], X[:, f], XN[:, f], ALU.add), [gat[g]], s=name)

            def stat(c):
                stt[c] = q.dve(lambda e: e.bn_stats(st[:, 6 * c:6 * c + 6], Xv[:, c, :]), [x2[c // 4]], s="bn")

            def aggregate(c):
                agg[c] = q.dve(lambda e: e.bn_aggr(mv[:, 2 * c:2 * c + 2], st[:, 6 * c:6 * c + 6]), [stt[c]], s="bn")

            def normalise(h, k, engines):
                rest = []
                f = slice(8 * h, 8 * h + 8)
                kb = q.dve(lambda e: e.scalar_tensor_tensor(
                    nt[:, f], mv[:, :].rearrange("p (c two) -> p c two", two=2)[:, f, 0], -1.0, rs[:, f],
                    ALU.mult, ALU.mult), [k], s="nw")
                for d in range(8 * h, 8 * h + 8):
                    eng = engines[d % 8]
                    if eng == "a":
                        xn2[d] = q.act(lambda e, d=d: e.activation(XNv[:, d, :], Xv[:, d, :], ACT.Identity,
                                                                   bias=nt[:, d:d + 1], scale=rs[:, d:d + 1]),
                                       [kb], s="xn2a")
                    else:
                        def apply(d=d):
                            xn2[d] = q.dve(lambda e: e.tensor_scalar(
                                XNv[:, d, :], Xv[:, d, :], mv[:, 2 * d:2 * d + 1], rs[:, d:d + 1],
                                ALU.subtract, ALU.mult), [k], s="xn2v")
                        rest.append(apply)
                return rest

            def turn_tiles(h):
                for g in range(2 * h, 2 * h + 2):
                    for d in range(4 * g, 4 * g + 4):
                        tp = q.pe(lambda e, d=d, g=g: e.transpose(PS[g][:, 128 * (d % 4):128 * (d % 4) + 128],
                                                                  XNv[:, d, :], ident[:, :]), [xn2[d]], s="tp")
                    tv2[g] = q.act(lambda e, g=g: e.activation(XNT[:, 512 * g:512 * g + 512], PS[g], ACT.Copy),
                                   [tp], s="ev")

            def landmarks(g):
                xb[g] = q.dve(lambda e: e.tensor_reduce(
                    XB[:, 8 * g:8 * g + 8], XNT[:, 512 * g:512 * g + 512].rearrange("p (m l) -> p m l", l=64),
                    AX, ALU.add), [tv2[g]], s="xb")

            add(0)
            add(1)
            add(2, q.pool, "x2p")
            add(3, q.pool, "x2p")
            for c in range(8):
                stat(c)
            for c in range(8):
                aggregate(c)
            other = [lambda c=c: stat(c) for c in range(8, 16)]
            for k in newton_steps(0, 8, [agg[7], warm]):
                if other:
                    other.pop(0)()
            for fn in other:
                fn()
            other = normalise(0, k, "aavavava")
            for c in range(8, 16):
                aggregate(c)
            for k in newton_steps(8, 16, [agg[15]]):
                if other:
                    other.pop(0)()
            turn_tiles(0)
            for fn in normalise(1, k, "avvavvav"):
                fn()
            turn_tiles(1)
            for g in range(4):
                landmarks(g)
            for d in range(16):
                xbias[d] = q.pool(lambda e, d=d: e.tensor_tensor(Xv[:, d, :], Xv[:, d, :], bfc[:, :], ALU.add),
                                  [xn2[d], lt], s="xbias")
            return x2[3]

        x2 = [None] * 16
        xn2, xbias, tv2, xb, gat, st2 = ({} for _ in range(6))
        XB = RP[:, 4096 + 1536:4096 + 1568]

        def attn1(tail):
            D1 = [RA[:, k:k + 512] for k in (8192, 8704, 9216, 15360)]
            AT = [RA[:, k:k + 512] for k in (9728, 10240, 10752, 15872)]
            CT = RA[:, 0:8192].rearrange("p (c n) -> p c n", c=4)
            E3 = [RP[:, 2048 * k:2048 * k + 2048] for k in range(2)]
            E3T = [RE[:, 2048 * k:2048 * k + 2048].rearrange("p (c n) -> p c n", c=16) for k in range(2)]
            A, B = RD[:, 1800:2312], RD[:, 2312:2824]
            BT = [RD[:, 2824 + 512 * k:3336 + 512 * k] for k in range(2)]
            F = RP[:, 4096:6144]
            a_, aT = F[:, 0:128], F[:, 128:256]
            ZZ = [F[:, 256:512], F[:, 512:768]]
            AZ, T1, T2, T3 = (F[:, 768 + 128 * k:896 + 128 * k] for k in range(4))
            AV = F[:, 1280:1536]
            sc2 = F[:, 1568:1600]
            AXT = sm[:, 0:512]
            ZT = sm[0:64, 512:1024]
            e2 = F[:, 1600:1728]
            G = RP[:, 0:512]
            ones_row = cst[0:1, 32:160]
            eye = cst[:, 160:192].unsqueeze(1).to_broadcast([128, 4, 32])
            def side(k, bank, bank2, dst, w):
                for j in range(4):
                    m = q.pe(lambda e, j=j: e.matmul(PS[bank][32 * j:32 * j + 32, :], XB, MM[k][:, j, :, :],
                                                     start=True, stop=True), w, s="sd")
                m = q.act(lambda e: e.activation(BT[k], PS[bank], ACT.Copy, scale=1.0 / 512), [m], s="sde")
                for c in range(4):
                    n = q.pe(lambda e, c=c: e.transpose(PS[bank2][:, 128 * c:128 * c + 128],
                                                        BT[k][:, 128 * c:128 * c + 128], ident[:, :]), [m], s="sdt")
                return q.act(lambda e: e.activation(dst, PS[bank2], ACT.Copy), [n], s="be")

            be = side(0, 2, 3, B, [xb[3], me[3]])
            for h in range(16):
                j, c = h % 4, h // 4
                s2 = q.pe(lambda e, h=h, j=j, c=c: e.matmul(
                    PS[7][32 * j:32 * j + 32, 32 * c:32 * c + 32], B[:, 32 * h:32 * h + 32], XB,
                    start=True, stop=True), [be], s="s2")

            def tokens_side():
                return side(1, 4, 5, A, [])

            side_a = tokens_side()

            def c3(v):
                return v.rearrange("p (c n) -> p c n", n=32)

            def bc(v):
                return v.unsqueeze(2).to_broadcast([128, 4, 32])

            mx, nm, sums = sc2[:, 0:4], sc2[:, 4:8], sc2[:, 8:12]
            k1 = q.dve(lambda e: e.tensor_reduce(mx, c3(PS[7][:, 0:128]), AX, ALU.max), [s2], s="p0")
            k1 = q.dve(lambda e: e.tensor_tensor(c3(e2), c3(PS[7][:, 0:128]), bc(mx), ALU.subtract), [k1], s="p0")
            k2 = q.act(lambda e: e.activation(e2, e2, ACT.Exp, scale=1.0 / 64), [k1], s="p0a")
            k1 = q.dve(lambda e: e.tensor_reduce(sums, c3(e2), AX, ALU.add), [k2], s="p0")
            k1 = q.dve(lambda e: e.reciprocal(nm, sums), [k1], s="p0")
            k1 = q.dve(lambda e: e.tensor_tensor(c3(a_), c3(e2), bc(nm), ALU.mult), [k1], s="p0")
            k1 = q.dve(lambda e: e.transpose(aT, a_), [k1], s="p0")
            k1 = q.dve(lambda e: e.tensor_reduce(sc2[:, 12:16], c3(a_), AX, ALU.add), [k1], s="p0")
            k1 = q.dve(lambda e: e.tensor_reduce(sc2[:, 16:20], c3(aT), AX, ALU.add), [k1], s="p0")
            k1 = q.dve(lambda e: e.tensor_reduce(sc2[:, 20:22], sc2[:, 12:20].rearrange("p (z c) -> p z c", z=2),
                                                 AX, ALU.max), [k1], s="p0")
            inits = [k1]

            def start_sums():
                q.pe(lambda e: e.transpose(PS[7][0:1, 128:256], sc2[:, 20:21], ident[:, :]), [inits[0]])
                m = q.pe(lambda e: e.transpose(PS[7][0:1, 256:384], sc2[:, 21:22], ident[:, :]), s="p0p")
                k1 = q.dve(lambda e: e.tensor_reduce(sc2[0:1, 22:24], PS[7][0:1, 128:384].rearrange(
                    "p (z c) -> p z c", z=2), AX, ALU.max), [m], s="p0")
                k1 = q.dve(lambda e: e.tensor_tensor(sc2[0:1, 24:25], sc2[0:1, 22:23], sc2[0:1, 23:24], ALU.mult),
                           [k1], s="p0")
                inits[0] = q.dve(lambda e: e.reciprocal(sc2[0:1, 25:26], sc2[0:1, 24:25]), [k1], s="p0")

            def start_z():
                m = q.pe(lambda e: e.matmul(PS[7][:, 384:385], ones_row, sc2[0:1, 25:26], start=True, stop=True),
                         [inits[0], ld_c], s="p0p")
                k1 = q.dve(lambda e: e.tensor_copy(sc2[:, 26:27], PS[7][:, 384:385]), [m], s="p0")
                k1 = q.dve(lambda e: e.tensor_scalar(ZZ[0][:, 0:128], aT, sc2[:, 26:27], None, ALU.mult), [k1], s="p0")
                zs[0] = q.dve(lambda e: e.tensor_scalar(ZZ[0][:, 128:256], a_, sc2[:, 26:27], None, ALU.mult),
                              [k1], s="p0")

            zs = [None]

            def heads_mm(outcol, lhs, rhs, w):
                for h in range(16):
                    j, c = h % 4, h // 4
                    r = slice(32 * j, 32 * j + 32)
                    f = slice(32 * c, 32 * c + 32)
                    tok = q.pe(lambda e, r=r, f=f, c=c: e.matmul(
                        PS[7][r, outcol + 32 * c:outcol + 32 * c + 32], lhs[r, f], rhs[r, f], start=True, stop=True),
                        w, s="pm_" if h == 15 else None)
                return tok

            def pinv_stages():
                yield from (start_sums, start_z)
                for it in range(6):
                    z, z2 = ZZ[it % 2], ZZ[(it + 1) % 2]

                    def st1(z=z):
                        m = heads_mm(0, aT, z[:, 0:128], zs)
                        zs[0] = q.dve(lambda e: e.tensor_copy(AZ, PS[7][:, 0:128]), [m], s="pd")
                        zs[0] = q.dve(lambda e: e.scalar_tensor_tensor(c3(T1), eye, 7.0, c3(PS[7][:, 0:128]),
                                                                       ALU.mult, ALU.subtract), [m], s="pd")

                    def st2():
                        m = heads_mm(0, AZ, T1, zs)
                        zs[0] = q.dve(lambda e: e.scalar_tensor_tensor(c3(T2), eye, 15.0, c3(PS[7][:, 0:128]),
                                                                       ALU.mult, ALU.subtract), [m], s="pd")

                    def st3():
                        m = heads_mm(0, AZ, T2, zs)
                        x = q.dve(lambda e: e.scalar_tensor_tensor(c3(T1), eye, 13.0, c3(PS[7][:, 0:128]),
                                                                   ALU.mult, ALU.subtract), [m], s="pd")
                        zs[0] = q.dve(lambda e: e.tensor_scalar(T3, T1, 0.25, None, ALU.mult), [x], s="pd")

                    def st4(z=z, z2=z2):
                        m = heads_mm(0, z[:, 128:256], T3, zs)
                        x = q.dve(lambda e: e.tensor_copy(z2[:, 0:128], PS[7][:, 0:128]), [m], s="pd")
                        zs[0] = q.dve(lambda e: e.transpose(z2[:, 128:256], z2[:, 0:128]), [x], s="pd")
                    yield from (st1, st2, st3, st4)

            ex, evt, axe, ave, rc = {}, {}, {}, {}, {}
            s3_, tt_, ax_ = {}, {}, {}
            sums3, rec3, nm3 = sc2[:, 27:31], sm[:, 1024:1028], sm[:, 1028:1032]

            def landmark_scores(c, gs):
                for g in gs:
                    s3_[c] = q.pe(lambda e, g=g: e.matmul(PS[g], B[:, 128 * c:128 * c + 128],
                                                          XNT[:, 512 * g:512 * g + 512], start=True, stop=True),
                                  [be, evt.get((c - 1, g))], s="s3")
                if gs[-1] == 3:
                    mxx = q.dve(lambda e: e.tensor_reduce(nm3[:, c:c + 1], PSA[:, 0:2048], AX, ALU.max, negate=True),
                                [s3_[c]], s="mx3")
                    ex[c] = q.act(lambda e: e.activation(E3[c % 2], PSA[:, 0:2048], ACT.Exp, bias=nm3[:, c:c + 1],
                                                         accum_out=sums3[:, c:c + 1]), [mxx, tt_.get(c - 2)], s="ex3")

            def landmark_turn(c):
                for g in range(4):
                    for k in range(4):
                        kk = 4 * g + k
                        tt_[c] = q.pe(lambda e, g=g, k=k, kk=kk: e.transpose(
                            PS[g][:, 128 * k:128 * k + 128], E3[c % 2][:, 128 * kk:128 * kk + 128], ident[:, :]),
                            [ex[c]], s="tt3")
                    v = E3T[c % 2][:, 4 * g:4 * g + 4, :]
                    if g % 2:
                        evt[c, g] = q.act(lambda e, g=g, v=v: e.activation(
                            v, PS[g].rearrange("p (k n) -> p k n", k=4), ACT.Copy), [tt_[c], ax_.get(c - 2)], s="evt1")
                    else:
                        evt[c, g] = q.dve(lambda e, g=g, v=v: e.tensor_copy(
                            v, PS[g].rearrange("p (k n) -> p k n", k=4)), [tt_[c], ax_.get(c - 2)], s="evt0")
                rc[c] = q.dve(lambda e: e.reciprocal(rec3[:, c:c + 1], sums3[:, c:c + 1]), [ex[c]], s="rc3")

            def landmark_tokens(c, kks):
                for kk in kks:
                    ax_[c] = q.pe(lambda e, kk=kk: e.matmul(PS[4][:, 128 * c:128 * c + 128], XNv[:, kk, :],
                                                            E3T[c % 2][:, kk, :], start=kk == 0, stop=kk == 15),
                                  [evt[c, kk // 4], ave.get(c - 1)], s="ax")
                if kks[-1] == 15:
                    axe[c] = q.act(lambda e: e.activation(AXT[:, 128 * c:128 * c + 128],
                                                          PS[4][:, 128 * c:128 * c + 128], ACT.Copy), [ax_[c]], s="axe")

            def landmark_values(c):
                for j in range(4):
                    h = 4 * c + j
                    av = q.pe(lambda e, j=j, h=h: e.matmul(PS[4][32 * j:32 * j + 32, 0:64], AXT[:, 32 * h:32 * h + 32],
                                                           WV[:, 64 * h:64 * h + 64], start=True, stop=True),
                              [axe[c], lw], s="av")
                ave[c] = q.dve(lambda e: e.tensor_scalar(AV[:, 64 * c:64 * c + 64], PS[4][:, 0:64],
                                                         rec3[:, c:c + 1], None, ALU.mult), [av, rc[c]], s="ave")

            M1 = [sm[:, 1040 + 16 * k:1056 + 16 * k] for k in range(4)]
            R1_ = [sm[:, 1104 + 16 * k:1120 + 16 * k] for k in range(4)]
            rec_, e1_, at_, sb1, cv_, cte = {}, {}, {}, {}, {}, {}
            NW = 18
            tok_a = [side_a]

            def window(w):
                a = 116 * w if w < 17 else 1920
                lo = 0 if w == 0 else 6 if w < 17 else 58
                return a, lo, 128 if w == 17 else 122

            def token_scores(w):
                a = window(w)[0]
                m = q.pe(lambda e: e.matmul(PS[5], XNT[:, a:a + 128], A, start=True, stop=True),
                         [tok_a[0], sb1.get(w - 1)], s="s1")
                bv = PS[5].rearrange("p (h n) -> p h n", n=32)
                dv = D1[w % 4].rearrange("p (h n) -> p h n", n=32)
                m1, r1_ = M1[w % 4], R1_[w % 4]

                def bh(v):
                    return v.unsqueeze(2).to_broadcast([128, 16, 32])
                k1 = q.dve(lambda e: e.tensor_reduce(m1, bv, AX, ALU.max), [m, rec_.get(w - 4)], s="d1")
                sb1[w] = q.dve(lambda e: e.tensor_tensor(dv, bv, bh(m1), ALU.subtract), [k1, at_.get(w - 4)], s="d1")
                e1_[w] = q.act(lambda e: e.activation(D1[w % 4], D1[w % 4], ACT.Exp), [sb1[w]], s="e1")

            def token_weights(w):
                dv = D1[w % 4].rearrange("p (h n) -> p h n", n=32)
                m1, r1_ = M1[w % 4], R1_[w % 4]
                k1 = q.dve(lambda e: e.tensor_reduce(m1, dv, AX, ALU.add), [e1_[w]], s="d1")
                k1 = rec_[w] = q.dve(lambda e: e.reciprocal(r1_, m1), [k1, at_.get(w - 4)], s="d1")
                at_[w] = q.pool(lambda e: e.tensor_tensor(
                    AT[w % 4].rearrange("p (h n) -> p h n", n=32), dv,
                    r1_.unsqueeze(2).to_broadcast([128, 16, 32]), ALU.mult), [k1, cv_.get(w - 4)], s="at1")

            def convolve(w):
                a, lo, hi = window(w)
                n = hi - lo
                for c in range(4):
                    for j in range(4):
                        h = 4 * c + j
                        cv_[w] = q.pe(lambda e, h=h, j=j, c=c: e.matmul(
                            PS[6][32 * j:32 * j + 32, 128 * c:128 * c + n], AT[w % 4][:, 32 * h:32 * h + 32],
                            TZ[:, h, lo + 6:hi + 6], start=True, stop=True), [at_[w], tz_[0], cte.get(w - 1)], s="cv")
                cte[w] = q.act(lambda e: e.activation(
                    CT[:, :, a + lo:a + hi], PS[6].rearrange("p (c n) -> p c n", c=4)[:, :, 0:n], ACT.Copy),
                    [cv_[w]], s="cte")

            main = []
            for c in range(4):
                main.append(lambda c=c: landmark_scores(c, (0, 1)))
                main.append(lambda c=c: landmark_scores(c, (2, 3)))
                if c == 0:
                    main += [lambda: None] * 1
                if c:
                    main.append(lambda c=c: landmark_tokens(c - 1, range(0, 8)))
                    main.append(lambda c=c: landmark_tokens(c - 1, range(8, 16)))
                main.append(lambda c=c: landmark_turn(c))
                if c:
                    main.append(lambda c=c: landmark_values(c - 1))
            main.append(lambda: landmark_tokens(3, range(0, 8)))
            main.append(lambda: landmark_tokens(3, range(8, 16)))
            main.append(lambda: None)
            main.append(lambda: landmark_values(3))
            stages = list(pinv_stages())

            def windows():
                for w in range(NW + 3):
                    def step(w=w):
                        if w < NW:
                            token_scores(w)
                        if 1 <= w <= NW:
                            token_weights(w - 1)
                        if w >= 3:
                            convolve(w - 3)
                    yield step
            wins = list(windows())
            zte, ge = {}, [None]

            def value_products():
                zs_last[0] = zs[0]
                for j in range(4):
                    for c in range(4):
                        r = slice(32 * j, 32 * j + 32)
                        zt = q.pe(lambda e, r=r, j=j, c=c: e.matmul(
                            PS[j][0:64, 32 * c:32 * c + 32], AV[r, 64 * c:64 * c + 64],
                            ZZ[0][r, 128 + 32 * c:160 + 32 * c], start=True, stop=True),
                            [zs[0], ave[3], evt[3, 0], evt[3, 1], evt[3, 2], evt[3, 3]], s="zt")
                    zte[j] = q.act(lambda e, j=j: e.activation(ZT[:, 128 * j:128 * j + 128], PS[j][0:64, 0:128],
                                                               ACT.Copy), [zt, ave[3]], s="zte")

            def output_products():
                for h in range(16):
                    j, c = h % 4, h // 4
                    gm = q.pe(lambda e, h=h, j=j, c=c: e.matmul(
                        PS[4][32 * j:32 * j + 32, 128 * c:128 * c + 128], ZT[:, 128 * j + 32 * c:128 * j + 32 * c + 32],
                        WF[:, h, :], start=True, stop=True), [zte[j], ave[3], lt], s="gm")
                ge[0] = q.dve(lambda e: e.tensor_copy(G, PS[4]), [gm, tt_[3], tt_[2]], s="ge")

            def final(c):
                b = PS[c % 4]
                w = min(NW - 1, max(0, -(-(128 * (c + 1) - 122) // 116)))
                for k in range(4):
                    fm = q.pe(lambda e, k=k: e.matmul(b[:, 0:128], CT[:, k, 128 * c:128 * c + 128],
                                                      G[:, 128 * k:128 * k + 128], start=k == 0, stop=k == 3),
                              [ge[0], cte[w], x3.get(c - 4), zte[3]], s="fm")
                x3[c] = q.dve(lambda e: e.tensor_tensor(Xv[:, c, :], b[:, 0:128], Xv[:, c, :], ALU.add),
                              [fm, xbias[c]], s="x3")

            landmarks_end = len(main)
            main += [value_products, lambda: None, output_products, lambda: None] + tail(final)
            ahead = [0, 0, 0]
            streams = [main, stages, wins]
            ends = [len(main), landmarks_end + SEND, landmarks_end + WEND]
            leads = [0, 0, WLEAD]
            for n in range(len(main)):
                for k, x in enumerate(streams):
                    while ahead[k] < min(len(x), (n + 1 + leads[k]) * len(x) // (ends[k] + leads[k])):
                        x[ahead[k]]()
                        ahead[k] += 1

        x3, zs_last = {}, [None]
        NSTEP = 4
        WEND, SEND, WLEAD = 8, 0, 1

        def ffn1():
            F = RP
            SG = [F[:, 512 + 576 * k:1088 + 576 * k] for k in range(2)]
            H = [F[:, 1664 + 576 * k:2240 + 576 * k] for k in range(2)]
            HT = [F[:, 2816 + 640 * k:3456 + 640 * k] for k in range(2)]
            pr, oh, p2, cw = (F[:, 4096 + 128 * k:4224 + 128 * k] for k in range(4))
            m1, m2 = F[:, 4608:4624], F[:, 4624:4640]
            later, st3, xn3, tv, lm, lgr, cwd = [], {}, {}, {}, {}, {}, {}

            def step(k=2):
                while later and k:
                    if next(later[0], "end") == "end":
                        later.pop(0)
                    else:
                        later.append(later.pop(0))
                    k -= 1

            bst = {}

            def finish(c, final):
                if c < 16:
                    final(c)
                if 1 <= c <= 16:
                    bst[c - 1] = q.dve(lambda e: e.bn_stats(st[:, 6 * (c - 1):6 * c], Xv[:, c - 1, :]),
                                       [x3[c - 1]], s="bn")
                if c >= 2:
                    st3[c - 2] = q.dve(lambda e: e.bn_aggr(mv[:, 2 * (c - 2):2 * (c - 2) + 2],
                                                           st[:, 6 * (c - 2):6 * (c - 2) + 6]), [bst[c - 2]], s="bn")
                    if c % 4 == 1:
                        later.append(norms3((c - 2) // 4))
                step(NSTEP)

            def norms3(g):
                for k in newton_steps(4 * g, 4 * g + 4, [st3[4 * g + 3]]):
                    yield
                for d in range(4 * g, 4 * g + 4):
                    xn3[d] = layernorm_apply(d, [k])
                    yield

            def turn_norms(g, bank=4):
                while 4 * g + 3 not in xn3:
                    step(1)
                for d in range(4 * g, 4 * g + 4):
                    tp = q.pe(lambda e, d=d: e.transpose(PS[bank][:, 128 * (d % 4):128 * (d % 4) + 128], XNv[:, d, :],
                                                         ident[:, :]), [xn3[d], tv.get(g - 1)], s="tp")
                tv[g] = q.act(lambda e: e.activation(XNT[:, 512 * g:512 * g + 512], PS[bank], ACT.Copy), [tp], s="ev")

            def logits(g):
                for d in range(4 * g, 4 * g + 4):
                    lm[g] = q.pe(lambda e, d=d: e.matmul(PS[7][:, 128 + 8 * d:136 + 8 * d], XNTv[:, d, :],
                                                         W3[:, 1152:1160], start=True, stop=True),
                                 [tv[g], lw3, zs_last[0], lgr.get(0)], s="lm")
                if g % 2:
                    later.append(router(g // 2))

            def router(z):
                f = slice(64 * z, 64 * z + 64)
                a, b = m1[:, 8 * z:8 * z + 8], m2[:, 8 * z:8 * z + 8]
                lg, pr_, oh_, p2_, cw_ = PS[7][:, 128 + 64 * z:192 + 64 * z], pr[:, f], oh[:, f], p2[:, f], cw[:, f]
                w8 = cst[:, 0:8].unsqueeze(1).to_broadcast([128, 8, 8])

                def e3(v):
                    return v.rearrange("p (c e) -> p c e", e=8)

                def b8(v):
                    return v.unsqueeze(2).to_broadcast([128, 8, 8])
                name = f"r2{z}"
                k = q.dve(lambda e: e.tensor_reduce(a, e3(lg), AX, ALU.max), [lm[2 * z + 1]], s=name)
                yield
                k = lgr[z] = q.dve(lambda e: e.tensor_tensor(e3(pr_), e3(lg), b8(a), ALU.subtract), [k], s=name)
                yield
                k = q.act(lambda e: e.activation(pr_, pr_, ACT.Exp), [k], s="p0a")
                for fn in (
                    lambda e: e.tensor_reduce(a, e3(pr_), AX, ALU.add),
                    lambda e: e.reciprocal(b, a),
                    lambda e: e.tensor_tensor(e3(pr_), e3(pr_), b8(b), ALU.mult),
                    lambda e: e.tensor_copy(p2_, pr_),
                ):
                    k = q.dve(fn, [k], s=name)
                    yield
                for r in range(2):
                    for fn in (
                        lambda e: e.tensor_reduce(a, e3(p2_), AX, ALU.max),
                        lambda e: e.tensor_tensor(e3(oh_), e3(p2_), b8(a), ALU.is_equal),
                        lambda e: e.tensor_tensor(e3(oh_), e3(oh_), w8, ALU.mult),
                        lambda e: e.tensor_reduce(b, e3(oh_), AX, ALU.max),
                        lambda e: e.tensor_tensor(e3(oh_), w8, b8(b), ALU.is_equal),
                        *((lambda e: e.tensor_tensor(cw_, oh_, pr_, ALU.mult),
                           lambda e: e.scalar_tensor_tensor(p2_, oh_, -4.0, p2_, ALU.mult, ALU.add)) if r == 0 else
                          (lambda e: e.tensor_tensor(oh_, oh_, pr_, ALU.mult),
                           lambda e: e.tensor_tensor(cw_, cw_, oh_, ALU.add))),
                    ):
                        k = q.dve(fn, [k], s=name)
                        yield
                cwd[z] = k
            sg, hh, hw, ht, he, dd, x4 = ({} for _ in range(7))

            def up(n):
                bg, bu, bs = PS[n % 2], PS[2 + n % 2], PS[4]
                x = XNTv[:, n, :]
                q.pe(lambda e: e.matmul(bg, x, W3[:, 0:512], start=True, stop=True),
                     [tv[n // 4], x3[12], x3[13], x3[14], x3[15], sg.get(n - 2), hh.get(n - 2)])
                g = q.pe(lambda e: e.matmul(bs[:, 0:128], x, W3[:, 1024:1152], start=True, stop=True),
                         [hh.get(n - 1), sg.get(n - 1), tv[2]], s="g2")
                u = q.pe(lambda e: e.matmul(bu, x, W3[:, 512:1024], start=True, stop=True), s="g2")
                q.act(lambda e: e.activation(SG[n % 2][:, 0:512], bg, ACT.Silu), [g, hh.get(n - 2)], s="sg2")
                sg[n] = q.act(lambda e: e.activation(SG[n % 2][:, 512:576], bs[:, 0:64], ACT.Silu), s="sg2")
                q.dve(lambda e: e.tensor_tensor(H[n % 2][:, 512:576], SG[n % 2][:, 512:576], bs[:, 64:128], ALU.mult),
                      [sg[n], u, ht.get(n - 2)], s="hh2")
                hh[n] = q.dve(lambda e: e.tensor_tensor(H[n % 2][:, 0:512], SG[n % 2][:, 0:512], bu, ALU.mult), s="hh2")
                hv = H[n % 2][:, 0:512].rearrange("p (e f) -> p e f", e=8)
                hw[n] = q.pool(lambda e: e.tensor_tensor(hv, hv, cw[:, 8 * n:8 * n + 8].unsqueeze(2).to_broadcast(
                    [128, 8, 64]), ALU.mult), [hh[n], cwd[n // 8]], s="hw2")

            def turn(n):
                for k in range(4):
                    q.pe(lambda e, k=k: e.transpose(PS[5][:, 128 * k:128 * k + 128],
                                                    H[n % 2][:, 128 * k:128 * k + 128], ident[:, :]),
                         [hw[n], he.get(n - 1), ("he2", n) if n else None, lgr[n // 8], lgr.get(1)])
                ht[n] = q.pe(lambda e: e.transpose(PS[7][0:64, 0:128], H[n % 2][:, 512:576], ident[:, :]), s="ht2")
                q.dve(lambda e: e.tensor_copy(HT[n % 2][0:64, 512:640], PS[7][0:64, 0:128]), [ht[n], dd.get(n - 2)], s="he2")
                he[n] = q.act(lambda e: e.activation(HT[n % 2][:, 0:512], PS[5], ACT.Copy), [ht[n], dd.get(n - 2)], s="he3")

            def down(n):
                s_ = q.count["he2"]
                for k in range(5):
                    K = 128 if k < 4 else 64
                    dd[n] = q.pe(lambda e, k=k, K=K: e.matmul(PS[6][:, 0:128], HT[n % 2][0:K, 128 * k:128 * k + 128],
                                                              D3[0:K, k, :], start=k == 0, stop=k == 4),
                                 [he[n], tv[3], ("he2", n + 1), x4.get(n - 1)], s="dd2")
                x4[n] = q.dve(lambda e: e.tensor_tensor(Xv[:, n, :], PS[6][:, 0:128], Xv[:, n, :], ALU.add),
                              [dd[n]], s="x4")
                a = {3: 0, 7: 4, 11: 8, 14: 12, 15: 15}.get(n)
                if a is not None:
                    dn.append(q.dma(out.rearrange("(c p) d -> p c d", p=128)[:, a:n + 1, :],
                                    Xv[:, a:n + 1, :], [x4[n]], s="out"))

            dn = []

            def tail(final):
                f = [lambda c=c: finish(c, final) for c in range(16)]
                f += [lambda: (finish(16, final), finish(17, final))]
                return [*f[0:10], lambda: turn_norms(0), *f[10:14], lambda: logits(0), lambda: turn_norms(1), *f[14:17],
                        lambda: logits(1), lambda: turn_norms(2)]

            attn1(tail)
            for n in range(18):
                if n == 0:
                    while 0 not in cwd:
                        step()
                if n == 1:
                    logits(2)
                    turn_norms(3, 6)
                    logits(3)
                    while 1 not in cwd:
                        step()
                if n < 16:
                    up(n)
                if 1 <= n <= 16:
                    turn(n - 1)
                if n >= 2:
                    down(n - 2)
            q.op("sync", lambda e: e.wait_ge(q.sems["out"], 80), [])

        if STOP == 1:
            dn = q.dma(out.rearrange("(c p) d -> p c d", p=128), Xv, [last], s="out")
            q.op("sync", lambda e: e.wait_ge(q.sems["out"], 16), [dn])

        if STOP >= 2:
            last = ffn0(last)
            if STOP == 2:
                dn = q.dma(out.rearrange("(c p) d -> p c d", p=128), Xv, [last], s="out")
                q.op("sync", lambda e: e.wait_ge(q.sems["out"], 16), [dn])
        if STOP >= 3:
            if STOP == 3:
                attn1(lambda final: [lambda c=c: final(c) for c in range(16)])
                dn = q.dma(out.rearrange("(c p) d -> p c d", p=128), Xv, [x3[15]], s="out")
                q.op("sync", lambda e: e.wait_ge(q.sems["out"], 16), [dn])
            else:
                ffn1()

        block = ctx.enter_context(nc.Block())

        @block.sync
        def _(e):
            q.emit("sync", e)

        @block.tensor
        def _(e):
            q.emit("tensor", e)

        @block.vector
        def _(e):
            q.emit("vector", e)

        @block.scalar
        def _(e):
            q.emit("scalar", e)

        @block.gpsimd
        def _(e):
            q.emit("gpsimd", e)


def layouts(inputs):
    import numpy as np

    f32 = np.float32
    a = {k: np.asarray(v) for k, v in inputs.items()}
    t = {}
    t["x"] = a["L0_attn_x"].reshape(2048, 128)
    t["ident"] = np.eye(128, dtype=f32)
    t["wqk"] = np.concatenate([a["L0_attn_Wq"].T, a["L0_attn_Wk"].T], 1)
    t["wv"] = a["L0_attn_Wv"].T.reshape(128, 8, 2, 8).transpose(0, 2, 1, 3).reshape(128, 128)
    t["wo"] = a["L0_attn_Wo"].T
    p = np.arange(128)
    col = np.arange(64)
    kl = (p % 64)[:, None]
    t["mask"] = np.concatenate([(col[None] > kl), (col[None] <= kl)], 1).astype(f32)
    slopes = np.power(f32(2.0), -(f32(8.0) * np.linspace(0.0, 1.0, 16, dtype=f32))).astype(f32)

    def parts(v):
        v = v.astype(f32)
        h = (v.view(np.uint32) & 0xFFFF0000).astype(np.uint32).view(f32)
        r = v - h
        m = (r.view(np.uint32) & 0xFFFF0000).astype(np.uint32).view(f32)
        return [h, m, r - m]

    st = np.zeros((128, 3, 2, 16, 16), f32)
    for k in range(3):
        ph = (2 * k + (p >= 64)) % 3
        for z, v in enumerate(parts(slopes[None] * (p % 64)[:, None])):
            st[:, k, 0, :, z] = v
            st[:, k, 1, :, z] = 1
        for z, v in enumerate(parts(-slopes[None] * (p % 64)[:, None])):
            st[:, k, 0, :, 3 + z] = 1
            st[:, k, 1, :, 3 + z] = v
        for r in range(3):
            d = (ph - r) % 3
            for z, v in enumerate(parts(-slopes[None] * (64 * d)[:, None])):
                st[:, k, 0, :, 6 + 3 * r + z] = (ph == r)[:, None]
                st[:, k, 1, :, 6 + 3 * r + z] = v
    t["stack"] = st.reshape(128, 1536)
    gu = np.concatenate([a["L0_ffn_gate_w"], a["L0_ffn_up_w"]], 1)
    t["gu"] = gu.transpose(2, 0, 1).reshape(128, 8 * 704)
    dw = np.zeros((8, 384, 128), f32)
    dw[:, :352] = a["L0_ffn_down_w"].transpose(0, 2, 1)
    t["dw"] = dw.reshape(8, 3, 128, 128).transpose(2, 0, 1, 3).reshape(128, 3072)
    t["rt"] = a["L0_ffn_router_w"].T
    cst = np.zeros((128, 360), f32)
    cst[:, 320:336] = np.arange(128)[:, None] + 128 * np.arange(16)[None] + 1
    cst[:, 336:359] = np.arange(128)[:, None] + 128 * np.arange(NTS)[None] + 2049
    e = np.arange(8)
    cst[:, 192:256] = 128.0 * (e[None] <= e[:, None]).reshape(64)
    cst[:, 256:320] = 128.0 * (e[None] < e[:, None]).reshape(64)
    cst[:, 32:160] = 1
    cst[:, 160:192] = np.arange(32)[None] == (p % 32)[:, None]
    cst[:, 0:8] = 8 - np.arange(8)
    cst[:, 8:31] = 128 * np.arange(23)
    t["cst"] = cst
    w = a["L1_attn_w_qkv"]
    t["w1"] = w[:, 2048:3072]
    t["wqT"] = w[:, 0:1024].T.reshape(16, 64, 128).transpose(1, 0, 2)
    t["wkT"] = w[:, 1024:2048].T.reshape(16, 64, 128).transpose(1, 0, 2)
    t["wf"] = a["L1_attn_w_fc"].reshape(16, 64, 128).transpose(1, 0, 2)
    t["bfc"] = np.broadcast_to(a["L1_attn_b_fc"][None], (128, 128))
    tz = np.zeros((128, 16, 140), f32)
    for k in range(13):
        tz[p, :, p + 12 - k] = a["L1_attn_w_conv"][:, 0, k, 0][None]
    t["tz"] = tz
    t["w3"] = np.concatenate([a["L1_ffn_wg"].reshape(512, 128).T, a["L1_ffn_wu"].reshape(512, 128).T,
                              a["L1_ffn_sg"].T, a["L1_ffn_su"].T, a["L1_ffn_gate_w"].T], 1)
    d3 = np.zeros((640, 128), f32)
    d3[:512] = a["L1_ffn_wd"].transpose(0, 2, 1).reshape(512, 128)
    d3[512:576] = a["L1_ffn_sd"].T
    t["d3"] = d3.reshape(5, 128, 128).transpose(1, 0, 2)
    t["tri"] = np.concatenate([np.triu(np.ones((128, 128)), 1), np.ones((128, 128))], 1).astype(f32)
    return {k: np.ascontiguousarray(v) for k, v in t.items()}


def kernel(**inputs):
    import concourse.bacc as _bacc
    from concourse.bass_utils import run_bass_kernel_spmd as _run

    arrays = layouts(inputs)
    nc = _bacc.Bacc("TRN2", target_bir_lowering=False, num_devices=1)
    t = {k: nc.dram_tensor(f"in_{k}", v.shape, mybir.dt.from_np(v.dtype), kind="ExternalInput").ap()
         for k, v in arrays.items()}
    out = nc.dram_tensor("out_0", (2048, 128), F32, kind="ExternalOutput").ap()
    build(nc, t, out)
    r = _run(nc, [{f"in_{k}": v for k, v in arrays.items()}], core_ids=[0])
    return r.results[0]["out_0"].reshape(1, 2048, 128)
```
